# Optimizing a Trainium2 kernel written in Bass

```python
import numpy as np
import jax
import jax.numpy as jnp

def _softmax(x, axis=-1):
    return jax.nn.softmax(x, axis=axis)

def _gelu(x):
    return jax.nn.gelu(x, approximate=True)

def _silu(x):
    return jax.nn.silu(x)

def _sigmoid(x):
    return jax.nn.sigmoid(x)

def _layernorm(x, axis=-1, eps=1e-05):
    m = jnp.mean(x, axis=axis, keepdims=True)
    v = jnp.var(x, axis=axis, keepdims=True)
    return (x - m) / jnp.sqrt(v + eps)

def _scatter_add(tgt, idx, src, axis=0):
    return tgt.at[idx].add(src)

def _segment_sum(src, seg, n):
    return jax.ops.segment_sum(src, seg, n)
kernel_name = 'mk_macaron_d1_jaxref_r8_08ded8'

def setup_inputs(seed: int=0):
    np.random.seed(seed)
    _w = jnp.asarray

    def _L0_attn_setup():
        import jax, jax.numpy as jnp
        import numpy as np
        B, SQ, HIDDEN = (2, 256, 256)
        HEADS, GROUPS, KVC = (16, 4, 128)
        HPG = HEADS // GROUPS
        LAYER_INDEX = 1
        SCALE = KVC ** (-0.5)
        key = jax.random.key(seed)
        k1, k2, k3, k4 = jax.random.split(key, 4)
        return {'x': jax.random.normal(k1, (B, SQ, HIDDEN), jnp.float32), 'w_q': jax.random.normal(k2, (HIDDEN, HEADS * KVC), jnp.float32) * 0.02, 'w_kv': jax.random.normal(k3, (HIDDEN, 2 * GROUPS * KVC), jnp.float32) * 0.02, 'w_dense': jax.random.normal(k4, (HEADS * KVC, HIDDEN), jnp.float32) * 0.02}
    _L0_attn_in = _L0_attn_setup()

    def _L0_ffn_setup():
        import jax, jax.numpy as jnp
        import numpy as np
        MIN_EXPERTS = 2
        NEG_INF = -1000000000.0

        def _l2norm(x, axis):
            return x / jnp.maximum(jnp.linalg.norm(x, axis=axis, keepdims=True), 1e-12)

        def _ste(x):
            return x + jax.lax.stop_gradient((x > 0).astype(x.dtype) - x)

        def _forward(hidden_states, sim_matrix, gates, q_proj, k_proj, v_proj, o_proj):
            B, T, C = hidden_states.shape
            E = gates.shape[0]
            H = q_proj.shape[-1]
            x = hidden_states.reshape(B * T, C)
            logits = _l2norm(x, -1) @ _l2norm(sim_matrix, 0) - jax.nn.sigmoid(gates)
            gated = jax.nn.relu(logits)
            mask = _ste(gated)
            inactive = jnp.sum(mask, axis=1) == 0
            fb_idx = jax.lax.top_k(logits, MIN_EXPERTS)[1]
            fb_mask = jnp.max(jax.nn.one_hot(fb_idx, E, dtype=mask.dtype), axis=1)
            mask = jnp.where(inactive[:, None] & (fb_mask > 0), jnp.ones_like(mask), mask)
            masked_logits = jnp.where(mask > 0, gated, jnp.full_like(gated, NEG_INF))
            probs = jax.nn.softmax(masked_logits, axis=-1)
            w = probs * (mask > 0)

            def mix(proj):
                pe = jnp.einsum('nc,ech->neh', x, proj)
                return jnp.einsum('ne,neh->nh', w, pe).reshape(B, T, H)
            q, k, v = (mix(q_proj), mix(k_proj), mix(v_proj))
            scale = 1.0 / jnp.sqrt(jnp.asarray(H, dtype=q.dtype))
            scores = jnp.einsum('bqh,bkh->bqk', q, k) * scale
            causal = jnp.tril(jnp.ones((T, T), dtype=bool))
            scores = jnp.where(causal[None], scores, jnp.full_like(scores, NEG_INF))
            attn = jax.nn.softmax(scores, axis=-1)
            ao = jnp.einsum('bqk,bkh->bqh', attn, v).reshape(B * T, H)
            wa = jnp.einsum('ne,nh->enh', w, ao)
            out = jnp.einsum('enh,ehc->nc', wa, o_proj)
            return out.reshape(B, T, C)
        key = jax.random.key(seed)
        ks = jax.random.split(key, 6)
        B, T, C, H, E = (4, 256, 256, 128, 16)
        xavier_qkv = float(np.sqrt(2.0 / (C + H)))
        return {'hidden_states': jax.random.normal(ks[0], (B, T, C), dtype=jnp.float32), 'sim_matrix': jax.random.normal(ks[1], (C, E), dtype=jnp.float32), 'gates': jnp.full((E,), -6.0, dtype=jnp.float32), 'q_proj': jax.random.normal(ks[2], (E, C, H), dtype=jnp.float32) * xavier_qkv, 'k_proj': jax.random.normal(ks[3], (E, C, H), dtype=jnp.float32) * xavier_qkv, 'v_proj': jax.random.normal(ks[4], (E, C, H), dtype=jnp.float32) * xavier_qkv, 'o_proj': jax.random.normal(ks[5], (E, H, C), dtype=jnp.float32) * xavier_qkv}
    _L0_ffn_in = _L0_ffn_setup()
    _d = {'L0_attn_x': _L0_attn_in['x'], 'L0_attn_w_q': _L0_attn_in['w_q'], 'L0_attn_w_kv': _L0_attn_in['w_kv'], 'L0_attn_w_dense': _L0_attn_in['w_dense'], 'L0_ffn_sim_matrix': _L0_ffn_in['sim_matrix'], 'L0_ffn_gates': _L0_ffn_in['gates'], 'L0_ffn_q_proj': _L0_ffn_in['q_proj'], 'L0_ffn_k_proj': _L0_ffn_in['k_proj'], 'L0_ffn_v_proj': _L0_ffn_in['v_proj'], 'L0_ffn_o_proj': _L0_ffn_in['o_proj']}
    _x0 = _d['L0_attn_x']
    _d['L0_attn_x'] = jax.random.normal(jax.random.fold_in(jax.random.key(seed), 1), (8, 512, 256), dtype=_x0.dtype)
    del _x0
    return _d

def reference(L0_attn_x, L0_attn_w_q, L0_attn_w_kv, L0_attn_w_dense, L0_ffn_sim_matrix, L0_ffn_gates, L0_ffn_q_proj, L0_ffn_k_proj, L0_ffn_v_proj, L0_ffn_o_proj):

    def _L0_attn_ref(x, w_q, w_kv, w_dense):
        import jax, jax.numpy as jnp
        import numpy as np
        B, SQ, HIDDEN = (2, 256, 256)
        HEADS, GROUPS, KVC = (16, 4, 128)
        HPG = HEADS // GROUPS
        LAYER_INDEX = 1
        SCALE = KVC ** (-0.5)
        b, sq, _ = x.shape
        sk = sq
        q = jnp.einsum('bsh,he->bse', x, w_q).reshape(b, sq, GROUPS, HPG, KVC)
        kv = jnp.einsum('bsh,he->bse', x, w_kv)
        k, v = jnp.split(kv, 2, axis=-1)
        k = k.reshape(b, sk, GROUPS, KVC)
        v = v.reshape(b, sk, GROUPS, KVC)
        scores = jnp.einsum('bqgpd,bkgd->bgqpk', q, k) * (SCALE / LAYER_INDEX)
        scores = scores.astype(jnp.float32) * LAYER_INDEX
        causal = jnp.arange(sq)[:, None] >= jnp.arange(sk)[None, :]
        scores = jnp.where(causal[None, None, :, None, :], scores, -jnp.inf)
        probs = jax.nn.softmax(scores, axis=-1).astype(x.dtype)
        ctx = jnp.einsum('bgqpk,bkgd->bqgpd', probs, v).reshape(b, sq, HEADS * KVC)
        return jnp.einsum('bse,eh->bsh', ctx, w_dense)

    def _L0_ffn_ref(hidden_states, sim_matrix, gates, q_proj, k_proj, v_proj, o_proj):
        import jax, jax.numpy as jnp
        import numpy as np
        MIN_EXPERTS = 2
        NEG_INF = -1000000000.0

        def _l2norm(x, axis):
            return x / jnp.maximum(jnp.linalg.norm(x, axis=axis, keepdims=True), 1e-12)

        def _ste(x):
            return x + jax.lax.stop_gradient((x > 0).astype(x.dtype) - x)

        def _forward(hidden_states, sim_matrix, gates, q_proj, k_proj, v_proj, o_proj):
            B, T, C = hidden_states.shape
            E = gates.shape[0]
            H = q_proj.shape[-1]
            x = hidden_states.reshape(B * T, C)
            logits = _l2norm(x, -1) @ _l2norm(sim_matrix, 0) - jax.nn.sigmoid(gates)
            gated = jax.nn.relu(logits)
            mask = _ste(gated)
            inactive = jnp.sum(mask, axis=1) == 0
            fb_idx = jax.lax.top_k(logits, MIN_EXPERTS)[1]
            fb_mask = jnp.max(jax.nn.one_hot(fb_idx, E, dtype=mask.dtype), axis=1)
            mask = jnp.where(inactive[:, None] & (fb_mask > 0), jnp.ones_like(mask), mask)
            masked_logits = jnp.where(mask > 0, gated, jnp.full_like(gated, NEG_INF))
            probs = jax.nn.softmax(masked_logits, axis=-1)
            w = probs * (mask > 0)

            def mix(proj):
                pe = jnp.einsum('nc,ech->neh', x, proj)
                return jnp.einsum('ne,neh->nh', w, pe).reshape(B, T, H)
            q, k, v = (mix(q_proj), mix(k_proj), mix(v_proj))
            scale = 1.0 / jnp.sqrt(jnp.asarray(H, dtype=q.dtype))
            scores = jnp.einsum('bqh,bkh->bqk', q, k) * scale
            causal = jnp.tril(jnp.ones((T, T), dtype=bool))
            scores = jnp.where(causal[None], scores, jnp.full_like(scores, NEG_INF))
            attn = jax.nn.softmax(scores, axis=-1)
            ao = jnp.einsum('bqk,bkh->bqh', attn, v).reshape(B * T, H)
            wa = jnp.einsum('ne,nh->enh', w, ao)
            out = jnp.einsum('enh,ehc->nc', wa, o_proj)
            return out.reshape(B, T, C)
        return _forward(hidden_states, sim_matrix, gates, q_proj, k_proj, v_proj, o_proj)
    x = L0_attn_x
    x = x + 0.5 * _L0_ffn_ref(_layernorm(x, axis=-1), L0_ffn_sim_matrix, L0_ffn_gates, L0_ffn_q_proj, L0_ffn_k_proj, L0_ffn_v_proj, L0_ffn_o_proj)
    x = x + _L0_attn_ref(_layernorm(x, axis=-1), L0_attn_w_q, L0_attn_w_kv, L0_attn_w_dense)
    x = x + 0.5 * _L0_ffn_ref(_layernorm(x, axis=-1), L0_ffn_sim_matrix, L0_ffn_gates, L0_ffn_q_proj, L0_ffn_k_proj, L0_ffn_v_proj, L0_ffn_o_proj)
    return x

_drawn_inputs = setup_inputs


def setup_inputs(seed=0):
    import zlib

    import numpy as np

    out = dict(_drawn_inputs(seed))
    spreads = {'L0_ffn_gates': (-6.0, 0.6)}
    factors = {'L0_attn_w_q': 8.0,
     'L0_ffn_sim_matrix': 3.716,
     'L0_ffn_q_proj': 8.0,
     'L0_ffn_k_proj': 8.0,
     'L0_ffn_v_proj': 3.191,
     'L0_ffn_o_proj': 3.233}
    for name, (base, spread) in spreads.items():
        noise = np.random.default_rng([zlib.crc32(name.encode()), seed]).standard_normal(out[name].shape)
        drawn = base * np.exp(spread * noise) if base else spread * noise
        out[name] = jnp.asarray(drawn.astype(out[name].dtype))
    for name, factor in factors.items():
        out[name] = (out[name] * factor).astype(out[name].dtype)
    return out
```

```python
from contextlib import ExitStack

import concourse.bass as bass
from concourse import mybir

ALU = mybir.AluOpType
ACT = mybir.ActivationFunctionType
AX = mybir.AxisListType
F32 = mybir.dt.float32
F32R = mybir.dt.float32r
BF16 = mybir.dt.bfloat16

P = 128
B, SEQ, C = 8, 512, 256
CK = C // P
QT = SEQ // P
TILES = B * QT
E, H = 16, 128
HEADS, GROUPS, D = 16, 4, 128
PER = HEADS // GROUPS
LN_EPS = 1e-5
NORM_MIN = 1e-12
SCALE = float(H) ** -0.5
MASKED = -1e30

QKV = 3 * H
OG = E // 2
RING = 4
STAGE = 3


class Resident:
    pass


def reach(eng, sem, value):
    if not isinstance(value, int) or value > 0:
        eng.wait_ge(sem, value)


def settle(eng):
    eng.nop(nofuse=True)


def tile_of(x, T):
    if isinstance(T, int):
        return x[:, T, :]
    return x[:, bass.ds(T, 1), :].rearrange("p a c -> p (a c)")


def as_f32(ap):
    return ap.bitcast(F32)


def constants(nc, m, sim_matrix, gates):
    with ExitStack() as ctx:
        sim = ctx.enter_context(nc.sbuf_tensor("sim", [P, CK, E], F32))
        sq = ctx.enter_context(nc.sbuf_tensor("sim_sq", [P, CK, E], F32))
        ones = ctx.enter_context(nc.sbuf_tensor("ones", [P, P], F32))
        norm = ctx.enter_context(nc.sbuf_tensor("sim_norm", [P, E], F32))
        rnorm = ctx.enter_context(nc.sbuf_tensor("sim_rnorm", [P, E], F32))
        simn = ctx.enter_context(nc.sbuf_tensor("sim_unit", [P, CK, E], F32))
        gate = ctx.enter_context(nc.sbuf_tensor("gate_rows", [P, E], F32))
        sums = ctx.enter_context(nc.psum_tensor("sim_sums", [P, E], F32))
        loaded = ctx.enter_context(nc.semaphore("const_loaded"))
        filled = ctx.enter_context(nc.semaphore("const_filled"))
        squared = ctx.enter_context(nc.semaphore("sim_squared"))
        summed = ctx.enter_context(nc.semaphore("sim_summed"))
        clamped = ctx.enter_context(nc.semaphore("sim_clamped"))
        powered = ctx.enter_context(nc.semaphore("sim_powered"))
        unit = ctx.enter_context(nc.semaphore("sim_unit_ready"))
        hi = ctx.enter_context(nc.semaphore("sim_hi_ready"))
        gexp = ctx.enter_context(nc.semaphore("gate_exp_ready"))
        gsum = ctx.enter_context(nc.semaphore("gate_sum_ready"))
        block = ctx.enter_context(nc.Block())

        @block.sync
        def _(sp):
            sp.dma_start(sim[:], sim_matrix.rearrange("(k p) e -> p k e", p=P)).then_inc(loaded, 16)
            sp.dma_start(gate[:], gates.partition_broadcast(P)).then_inc(loaded, 16)

        @block.gpsimd
        def _(pool):
            pool.memset(ones[:], 1.0).then_inc(filled, 1)
            pool.memset(m.power[:], -0.5).then_inc(filled, 1)
            pool.memset(m.ident[:], 0.0).then_inc(filled, 1)
            pool.memset(m.ident_bf[:], 0.0).then_inc(filled, 1)
            pool.memset(m.mask[:], 0.0).then_inc(filled, 1)
            pool.iota(m.rank_i[:], pattern=[[-1, E]], base=E, channel_multiplier=0).then_inc(filled, 1)
            pool.wait_ge(filled, 6)
            for ident in (m.ident, m.ident_bf):
                pool.affine_select(out=ident[:], in_=ident[:], compare_op=ALU.not_equal, fill=1.0, base=0,
                                   pattern=[[-1, P]], channel_multiplier=1).then_inc(filled, 1)
            pool.affine_select(out=m.mask[:], in_=m.mask[:], compare_op=ALU.is_ge, fill=MASKED, base=0,
                               pattern=[[-1, P]], channel_multiplier=1).then_inc(filled, 1)
            pool.tensor_scalar(m.rank[:], m.rank_i[:], 1.0 / 64, None, ALU.mult).then_inc(filled, 1)
            pool.wait_ge(summed, 2)
            pool.tensor_scalar(norm[:], norm[:], NORM_MIN ** 2, None, ALU.max).then_inc(clamped, 1)
            pool.wait_ge(clamped, 1)
            pool.tensor_tensor(rnorm[:], norm[:], m.power[:, 0:E], ALU.pow).then_inc(powered, 1)
            pool.wait_ge(filled, 10)

        @block.tensor
        def _(pe):
            pe.wait_ge(filled, 1)
            pe.wait_ge(squared, 1)
            for k in range(CK):
                last = pe.matmul(sums[:], ones[:], sq[:, k], start=(k == 0), stop=(k == CK - 1))
            last.then_inc(summed, 1)

        @block.vector
        def _(dve):
            dve.wait_ge(loaded, 32)
            dve.tensor_tensor(sq[:], sim[:], sim[:], ALU.mult).then_inc(squared, 1)
            dve.wait_ge(gexp, 1)
            dve.tensor_scalar(gate[:], gate[:], 1.0, None, ALU.add).then_inc(gsum, 1)
            dve.wait_ge(gsum, 1)
            dve.reciprocal(m.sig[:], gate[:]).then_inc(gsum, 1)
            dve.wait_ge(summed, 1)
            dve.tensor_copy(norm[:], sums[:]).then_inc(summed, 1)
            dve.wait_ge(powered, 1)
            for k in range(CK):
                last = dve.tensor_tensor(simn[:, k], sim[:, k], rnorm[:], ALU.mult)
            last.then_inc(unit, 1)
            dve.wait_ge(hi, CK)
            for k in range(CK):
                last = dve.tensor_tensor(m.simw[:, k, E:2 * E], simn[:, k], as_f32(m.simw[:, k, 0:E]), ALU.subtract)

        @block.scalar
        def _(act):
            act.wait_ge(loaded, 32)
            act.activation(gate[:], gate[:], ACT.Exp, scale=-1.0).then_inc(gexp, 1)
            act.wait_ge(unit, 1)
            for k in range(CK):
                act.activation(m.simw[:, k, 0:E], simn[:, k], ACT.Copy).then_inc(hi, 1)


def ffn_slots(eng, slot):
    slot(0, 0)
    slot(1, 1)
    with eng.Fori(0, B - 1) as k:
        for s in range(2, 2 + QT):
            slot(k * QT + s, s % QT)
    for T in range(TILES - 2, TILES + 2):
        slot(T, T % QT)


def inside(T, lag):
    return not isinstance(T, int) or 0 <= T - lag < TILES


def mix_bank(T, e):
    return (e if not inside(T, 2) else e + e // 2) % RING


def out_bank(T, g):
    return (g if not inside(T, 0) else 3 * g + 2) % RING


def ffn(nc, m, name, first, q_proj, k_proj, v_proj, o_proj, x_in, out):
    with ExitStack() as ctx:
        def sb(n, shape, dt=F32):
            return ctx.enter_context(nc.sbuf_tensor(f"{name}_{n}", shape, dt))

        def ps(n):
            return ctx.enter_context(nc.psum_tensor(f"{name}_{n}", [P, 512], F32))

        def sem(n):
            return ctx.enter_context(nc.semaphore(f"{name}_{n}"))

        wm = sb("mix_weights", [P, E, 2, CK, QKV], F32R)
        wo = sb("out_weights", [P, OG, 2, 2 * C], F32R)
        stage = sb("weight_stage", [P, STAGE, CK * QKV])
        stats = sb("ln_stats", [P, 2, 6])
        mv = sb("ln_mean_var", [P, 2, 2])
        var_eps = sb("ln_var_eps", [P, 1])
        rstd = sb("ln_rstd", [P, 2])
        y = sb("y", [P, 2, C])
        y_sq = sb("y_squares", [P, C])
        y_ss = sb("y_sum_squares", [P, 2])
        y_ss_min = sb("y_ss_clamped", [P, 1])
        y_rn = sb("y_rnorm", [P, 2])
        yT = sb("yT", [P, 2, 2, C], F32R)
        dot = sb("gate_dots", [P, E])
        logit = sb("gate_logits", [P, E])
        top = sb("gate_top", [P, 8])
        at_second = sb("gate_at_second", [P, E])
        at_rank = sb("gate_at_rank", [P, E])
        at_first = sb("gate_at_first", [P, E])
        key = sb("gate_key", [P, E])
        key_top = sb("gate_key_top", [P, 8])
        idle = sb("gate_idle", [P, 1])
        neg_max = sb("gate_neg_max", [P, 1])
        gated = sb("gate_relu", [P, E])
        is_top = sb("gate_is_top", [P, E])
        fallback = sb("gate_fallback", [P, E])
        active = sb("gate_active", [P, E])
        chosen = sb("gate_chosen", [P, E])
        g_exp = sb("gate_exp", [P, E])
        g_kept = sb("gate_kept", [P, E])
        g_sum = sb("gate_sum", [P, 1])
        g_rsum = sb("gate_rsum", [P, 1])
        w = sb("w", [P, QT, E])
        w_out = sb("w_out", [P, 2, E])
        acc = sb("mix_sums", [P, 2, 2, QKV])
        qkv = sb("qkv", [P, QKV])
        qT = sb("qT", [P, 2, P], F32R)
        kT = sb("kT", [P, QT, 2, P], F32R)
        v = sb("v", [P, QT, 2, H], F32R)
        s_max = sb("score_neg_max", [P, 1])
        s_bias = sb("score_bias", [P, 1])
        prob = sb("prob", [P, SEQ])
        p_sum = sb("prob_sum", [P, 1])
        p_rsum = sb("prob_rsum", [P, 1])
        pT = sb("probT", [P, QT, 2, P], F32R)
        av_half = sb("av_half", [P, P])
        av = sb("av", [P, P])
        avT = sb("avT", [P, 2, 2, P], F32R)
        odd = sb("out_odd", [P, 2, C])

        ring = [ps(f"ring{i}") for i in range(RING)]
        tr = ps("transposes")
        sc = ps("scores")
        pt = ps("probs_av")

        x_first, x_rest = sem("x_first"), sem("x_rest")
        w_loaded = [sem(f"w_loaded{i}") for i in range(STAGE)]
        w_hi, w_lo = sem("w_hi"), sem("w_lo")
        stats_done, mv_done, var_done, rstd_done = sem("stats"), sem("mv"), sem("var_eps"), sem("rstd")
        y_done, ss_done, ss_min_done, rn_done = sem("y"), sem("y_ss"), sem("y_ss_min"), sem("y_rn")
        yT_tr, yT_hi, yT_lo = sem("yT_tr"), sem("yT_hi"), sem("yT_lo")
        dots_ready, dot_read, logit_done, top_done = sem("dots"), sem("dot_read"), sem("logit"), sem("top")
        pool_gate, key_top_done, g_exp_done = sem("pool_gate"), sem("key_top"), sem("g_exp")
        kept_done, rsum_done, w_done, w_out_done = sem("kept"), sem("g_rsum"), sem("w"), sem("w_out")
        mix_ready, mix_done, out_ready, out_done = sem("mix_rdy"), sem("mix_done"), sem("out_rdy"), sem("out_done")
        merged, v_hi, v_lo = sem("merged"), sem("v_hi"), sem("v_lo")
        qk_tr, qk_hi, qk_lo = sem("qk_tr"), sem("qk_hi"), sem("qk_lo")
        scores_ready, smax_done, sbias_done, exp_done = sem("scores_rdy"), sem("smax"), sem("sbias"), sem("exp")
        p_rsum_done = sem("p_rsum")
        pt_tr, pt_hi, pt_lo, av_ready = sem("pt_tr"), sem("pt_hi"), sem("pt_lo"), sem("av_rdy")
        av_half_done, av_done, av_hi, av_lo = sem("av_half"), sem("av"), sem("av_hi"), sem("av_lo")
        x_merged, stored = sem("x_merged"), sem("stored")

        block = ctx.enter_context(nc.Block())

        @block.sync
        def _(sp):
            def load(n, dst, src):
                reach(sp, w_lo, n - STAGE + 1)
                sp.dma_start(dst, src).then_inc(w_loaded[n % STAGE], 16)

            if first:
                x_rows = x_in.rearrange("b (t p) c -> p (b t) c", p=P)
                sp.dma_start(m.x[:, 0:QT, :], x_rows[:, 0:QT, :]).then_inc(x_first, 16)
            for e in range(E):
                for i, proj in enumerate((q_proj, k_proj, v_proj)):
                    dst = stage[:, e % STAGE].rearrange("p (k n) -> p k n", k=CK)[:, :, i * H:(i + 1) * H]
                    load(e, dst, proj[e].rearrange("(k p) h -> p k h", p=P))
            for g in range(OG):
                dst = stage[:, (E + g) % STAGE, 0:2 * C].rearrange("p (e c) -> p e c", e=2)
                load(E + g, dst, o_proj[2 * g:2 * g + 2].rearrange("e h c -> h e c"))
                if first and g == 0:
                    for b in range(1, B):
                        sp.dma_start(m.x[:, b * QT:(b + 1) * QT, :],
                                     x_rows[:, b * QT:(b + 1) * QT, :]).then_inc(x_rest, 16)
            if out is not None:
                out_rows = out.rearrange("b (t p) c -> b p t c", p=P)
                with sp.Fori(0, B) as b:
                    sp.wait_ge(x_merged, b * QT + QT)
                    sp.dma_start(out_rows[bass.ds(b, 1)].rearrange("a p t c -> p (a t) c"),
                                 m.x[:, bass.ds(b * QT, QT), :]).then_inc(stored, 16)
                sp.wait_ge(stored, 16 * B)

        def staged(eng, n):
            before = [0 if i >= n else (48 if i < E else 16) for i in range(n % STAGE, n, STAGE)]
            eng.wait_ge(w_loaded[n % STAGE], sum(before) + (48 if n < E else 16))

        def weight_halves(n):
            if n < E:
                return (stage[:, n % STAGE, :], wm[:, n, 0].rearrange("p k n -> p (k n)"),
                        wm[:, n, 1].rearrange("p k n -> p (k n)"))
            return stage[:, n % STAGE, 0:2 * C], wo[:, n - E, 0], wo[:, n - E, 1]

        def stage_of(T, e):
            if isinstance(T, int) and T == 0:
                return e
            if isinstance(T, int) and T == 1 and e % 2:
                return E + e // 2
            return None

        @block.tensor
        def _(pe):
            def bank_free(T, i):
                p = i - RING
                if not inside(T, 2):
                    reach(pe, mix_done, E * T + p + 1)
                elif not inside(T, 0) and (T > TILES or p >= 0):
                    pe.wait_ge(out_done, OG * (T - 2) + p + 1)
                elif p < 0:
                    if p == -1 and not inside(T, 0):
                        pe.wait_ge(out_done, OG * (T - 2))
                    else:
                        pe.wait_ge(mix_done, E * T + (-1, -1, 0, 1)[p])
                elif p % 3 == 2:
                    pe.wait_ge(out_done, OG * (T - 2) + p // 3 + 1)
                else:
                    pe.wait_ge(mix_done, E * T + p - p // 3 + 1)

            def transpose_y(T, t):
                pe.wait_ge(y_done, T + 1)
                reach(pe, qk_lo, T - 2)
                if isinstance(T, int) and T == 1:
                    pe.wait_ge(yT_lo, 1)
                for k in range(CK):
                    last = pe.transpose(tr[:, k * P:(k + 1) * P], y[:, t % 2, k * P:(k + 1) * P], m.ident[:])
                last.then_inc(yT_tr, 1)

            def gate_dots(T, t):
                pe.wait_ge(yT_hi, T + 1)
                pe.wait_ge(yT_lo, T + 1)
                reach(pe, dot_read, T)
                for k in range(CK):
                    for half in range(2):
                        last = pe.matmul(sc[:, 0:2 * E], yT[:, t % 2, half, k * P:(k + 1) * P], m.simw[:, k],
                                         start=(k == 0 and half == 0), stop=(k == CK - 1 and half == 1))
                last.then_inc(dots_ready, 1)

            def mix(T, t, e):
                if e == 0:
                    pe.wait_ge(yT_hi, T + 1)
                    pe.wait_ge(yT_lo, T + 1)
                if isinstance(T, int) and T == 0:
                    pe.wait_ge(w_lo, e + 1)
                bank_free(T, e if not inside(T, 2) else e + e // 2)
                bank = ring[mix_bank(T, e)]
                n = 0
                for k in range(CK):
                    for h, wh in ((0, 0), (1, 0), (0, 1)):
                        last = pe.matmul(bank[:, 0:QKV], yT[:, t % 2, h, k * P:(k + 1) * P], wm[:, e, wh, k],
                                         start=(n == 0), stop=(n == 3 * CK - 1))
                        n += 1
                last.then_inc(mix_ready, 1)

            def transpose_qk(T, t):
                pe.wait_ge(merged, 2 * T + 1)
                pe.wait_ge(yT_lo, (T + 3) if inside(T + 2, 0) else TILES)
                for i in range(2):
                    last = pe.transpose(tr[:, i * P:(i + 1) * P], qkv[:, i * H:(i + 1) * H], m.ident[:])
                last.then_inc(qk_tr, 1)

            def scores(T, t):
                n = (t + 1) * P
                pe.wait_ge(qk_hi, T + 1)
                pe.wait_ge(qk_lo, T + 1)
                pe.wait_ge(dot_read, (T + 3) if inside(T + 2, 0) else TILES)
                out_ap = sc[:, 0:n].rearrange("p (j k) -> p j k", k=P)
                for i, (h, kh) in enumerate(((0, 0), (1, 0), (0, 1))):
                    pe.matmul(out_ap, qT[:, h], kT[:, 0:t + 1, kh], start=(i == 0), stop=False)
                pe.matmul(sc[:, t * P:n], m.ident_bf[:], m.mask[:], start=False, stop=True).then_inc(scores_ready, 1)

            def transpose_probs(T, t):
                pe.wait_ge(exp_done, T + 1)
                reach(pe, av_done, T)
                for j in range(t + 1):
                    last = pe.transpose(pt[:, j * P:(j + 1) * P], prob[:, j * P:(j + 1) * P], m.ident[:])
                last.then_inc(pt_tr, 1)

            def attend(T, t):
                pe.wait_ge(pt_hi, T + 1)
                pe.wait_ge(pt_lo, T + 1)
                pe.wait_ge(v_lo, T + 1)
                for j in range(t + 1):
                    for half in range(2):
                        last = pe.matmul(pt[:, 0:2 * P], v[:, j, half], pT[:, j].rearrange("p h q -> p (h q)"),
                                         start=(j == 0 and half == 0), stop=(j == t and half == 1))
                last.then_inc(av_ready, 1)

            def project(T, t, g, bank):
                if g == 0:
                    pe.wait_ge(av_lo, T + 1)
                if isinstance(T, int) and T == 0:
                    pe.wait_ge(w_lo, E + g + 1)
                bank_free(T + 2, g if not inside(T + 2, 0) else 3 * g + 2)
                for i, (h, wh) in enumerate(((0, 0), (1, 0), (0, 1))):
                    last = pe.matmul(bank[:], avT[:, t % 2, h], wo[:, g, wh], start=(i == 0), stop=(i == 2))
                last.then_inc(out_ready, 1)

            def slot(T, t):
                for e in range(E):
                    if inside(T, 0):
                        mix(T, t, e)
                    if e % 2 and inside(T, 2):
                        project(T - 2, (t + 2) % QT, e // 2, ring[out_bank(T, e // 2)])
                    if e == 0 and inside(T, -1):
                        transpose_y(T + 1, (t + 1) % QT)
                    if e == 2 and inside(T, -1):
                        gate_dots(T + 1, (t + 1) % QT)
                    if e == 4 and inside(T, 1):
                        transpose_qk(T - 1, (t + 3) % QT)
                    if e == 6 and inside(T, 1):
                        scores(T - 1, (t + 3) % QT)
                    if e == 9 and inside(T, 1):
                        transpose_probs(T - 1, (t + 3) % QT)
                    if e == 12 and inside(T, 1):
                        attend(T - 1, (t + 3) % QT)

            transpose_y(0, 0)
            gate_dots(0, 0)
            ffn_slots(pe, slot)

        @block.vector
        def _(dve):
            def ln_stats(T, t):
                if first and isinstance(T, int) and T < QT:
                    dve.wait_ge(x_first, 16)
                elif first:
                    dve.wait_ge(x_rest, 16 * (B - 1))
                dve.bn_stats(stats[:, t % 2], tile_of(m.x, T)).then_inc(stats_done, 1)

            def ln_aggregate(T, t):
                dve.wait_ge(stats_done, T + 1)
                reach(dve, var_done, T - 1)
                settle(dve)
                dve.bn_aggr(mv[:, t % 2], stats[:, t % 2]).then_inc(mv_done, 1)

            def ln_apply(T, t):
                dve.wait_ge(rstd_done, T + 1)
                reach(dve, yT_tr, T - 1)
                reach(dve, ss_done, T - 1)
                dve.tensor_scalar(y[:, t % 2], tile_of(m.x, T), mv[:, t % 2, 0:1], rstd[:, t % 2:t % 2 + 1],
                                  ALU.subtract, ALU.mult).then_inc(y_done, 1)

            def split_y(T, t):
                dve.wait_ge(yT_hi, T + 1)
                dve.tensor_tensor(yT[:, t % 2, 1], tr[:, 0:C], as_f32(yT[:, t % 2, 0]), ALU.subtract).then_inc(yT_lo, 1)

            def gate_dot(T, t):
                dve.wait_ge(dots_ready, T + 1)
                dve.tensor_copy(dot[:], sc[:, E:2 * E]).then_inc(logit_done, 1)
                dve.wait_ge(logit_done, 3 * T + 1)
                dve.tensor_tensor(dot[:], sc[:, 0:E], dot[:], ALU.add).then_inc(dot_read, 1)

            def gate_logit(T, t):
                dve.wait_ge(dot_read, T + 1)
                dve.wait_ge(rn_done, T + 1)
                reach(dve, pool_gate, 9 * T)
                dve.scalar_tensor_tensor(logit[:], dot[:], y_rn[:, t % 2:t % 2 + 1], m.sig[:],
                                         ALU.mult, ALU.subtract).then_inc(logit_done, 1)

            def gate_top(T, t):
                dve.wait_ge(logit_done, 3 * T + 2)
                settle(dve)
                dve.max(top[:], logit[:]).then_inc(top_done, 1)

            def gate_key_top(T, t):
                dve.wait_ge(pool_gate, 9 * T + 6)
                settle(dve)
                dve.max(key_top[:], key[:]).then_inc(key_top_done, 1)

            def gate_kept(T, t):
                dve.wait_ge(pool_gate, 9 * T + 9)
                dve.wait_ge(g_exp_done, T + 1)
                dve.tensor_tensor(g_kept[:], g_exp[:], chosen[:], ALU.mult).then_inc(kept_done, 1)

            def gate_sum(T, t):
                dve.wait_ge(kept_done, T + 1)
                dve.tensor_reduce(g_sum[:], g_kept[:], AX.X, ALU.add).then_inc(logit_done, 1)

            def gate_rsum(T, t):
                dve.wait_ge(logit_done, 3 * T + 3)
                dve.reciprocal(g_rsum[:], g_sum[:]).then_inc(rsum_done, 1)

            def gate_weights(T, t):
                dve.wait_ge(rsum_done, T + 1)
                dve.tensor_scalar(w[:, t], g_kept[:], g_rsum[:, 0:1], None, ALU.mult).then_inc(w_done, 1)

            def sum_mix(T, t, e):
                into = acc[:, t % 2, e % 2]
                bank = ring[mix_bank(T, e)]
                if e == 0:
                    dve.wait_ge(w_done, T + 1)
                if e < 2:
                    reach(dve, merged, 2 * T - 2)
                else:
                    dve.wait_ge(mix_done, E * T + e - 1)
                dve.wait_ge(mix_ready, E * T + e + 1)
                if e < 2:
                    dve.tensor_scalar(into, bank[:, 0:QKV], w[:, t, e:e + 1], None, ALU.mult).then_inc(mix_done, 1)
                else:
                    dve.scalar_tensor_tensor(into, bank[:, 0:QKV], w[:, t, e:e + 1], into,
                                             ALU.mult, ALU.add).then_inc(mix_done, 1)

            def sum_output(T, t, g, bank):
                dve.wait_ge(out_ready, OG * T + g + 1)
                if g == 0:
                    dve.wait_ge(w_out_done, T + 1)
                    dve.wait_ge(merged, 2 * T + 1)
                else:
                    dve.wait_ge(out_done, OG * T + g)
                x = tile_of(m.x, T)
                wt = w_out[:, t % 2]
                dve.scalar_tensor_tensor(x, bank[:, 0:C], wt[:, 2 * g:2 * g + 1], x, ALU.mult, ALU.add)
                if g == 0:
                    dve.tensor_scalar(odd[:, t % 2], bank[:, C:2 * C], wt[:, 1:2], None, ALU.mult).then_inc(out_done, 1)
                else:
                    dve.scalar_tensor_tensor(odd[:, t % 2], bank[:, C:2 * C], wt[:, 2 * g + 1:2 * g + 2], odd[:, t % 2],
                                             ALU.mult, ALU.add).then_inc(out_done, 1)

            def split_qk(T, t):
                dve.wait_ge(qk_hi, T + 1)
                dve.tensor_tensor(qT[:, 1], tr[:, 0:P], as_f32(qT[:, 0]), ALU.subtract)
                dve.tensor_tensor(kT[:, t, 1], tr[:, P:2 * P], as_f32(kT[:, t, 0]), ALU.subtract).then_inc(qk_lo, 1)

            def score_max(T, t):
                dve.wait_ge(scores_ready, T + 1)
                dve.tensor_reduce(s_max[:], sc[:, 0:(t + 1) * P], AX.X, ALU.max).then_inc(smax_done, 1)
                dve.wait_ge(smax_done, T + 1)
                dve.tensor_scalar(s_bias[:], s_max[:], -SCALE, None, ALU.mult).then_inc(sbias_done, 1)

            def split_probs(T, t):
                n = (t + 1) * P
                dve.wait_ge(pt_hi, T + 1)
                dve.tensor_tensor(pT[:, 0:t + 1, 1], pt[:, 0:n].rearrange("p (j q) -> p j q", q=P),
                                  as_f32(pT[:, 0:t + 1, 0]), ALU.subtract).then_inc(pt_lo, 1)

            def prob_rsum(T, t):
                dve.wait_ge(exp_done, T + 1)
                dve.reciprocal(p_rsum[:], p_sum[:]).then_inc(p_rsum_done, 1)

            def output_weights(T, t):
                dve.wait_ge(p_rsum_done, T + 1)
                dve.tensor_scalar(w_out[:, t % 2], w[:, t], p_rsum[:, 0:1], 0.5, ALU.mult, ALU.mult).then_inc(w_out_done, 1)

            def sum_av(T, t):
                dve.wait_ge(av_ready, T + 1)
                dve.tensor_copy(av_half[:], pt[:, P:2 * P]).then_inc(av_half_done, 1)
                reach(dve, av_lo, T)
                dve.wait_ge(av_half_done, T + 1)
                dve.tensor_tensor(av[:], pt[:, 0:P], av_half[:], ALU.add).then_inc(av_done, 1)

            def split_weights(n):
                raw, hi, lo = weight_halves(n)
                dve.wait_ge(w_hi, n + 1)
                dve.tensor_tensor(lo, raw, as_f32(hi), ALU.subtract).then_inc(w_lo, 1)

            def slot(T, t):
                nxt, prev, nn = (t + 1) % QT, (t + 3) % QT, (t + 2) % QT
                for e in range(E):
                    if stage_of(T, e) is not None:
                        split_weights(stage_of(T, e))
                    if inside(T, 0):
                        sum_mix(T, t, e)
                    if e == 0 and inside(T, -1):
                        split_y(T + 1, nxt)
                    if e % 2 and inside(T, 2):
                        g = e // 2
                        sum_output(T - 2, nn, g, ring[out_bank(T, g)])
                    if inside(T, -2):
                        if e == 0:
                            ln_stats(T + 2, nn)
                        if e == 2:
                            ln_aggregate(T + 2, nn)
                        if e == 5:
                            ln_apply(T + 2, nn)
                    if inside(T, -1):
                        if e == 3:
                            gate_dot(T + 1, nxt)
                        if e == 4:
                            gate_logit(T + 1, nxt)
                        if e == 5:
                            gate_top(T + 1, nxt)
                        if e == 9:
                            gate_key_top(T + 1, nxt)
                        if e == 12:
                            gate_kept(T + 1, nxt)
                        if e == 13:
                            gate_sum(T + 1, nxt)
                        if e == 14:
                            gate_rsum(T + 1, nxt)
                        if e == 15:
                            gate_weights(T + 1, nxt)
                    if inside(T, 1):
                        if e == 4:
                            split_qk(T - 1, prev)
                        if e == 7:
                            score_max(T - 1, prev)
                        if e == 9:
                            prob_rsum(T - 1, prev)
                        if e == 10:
                            split_probs(T - 1, prev)
                        if e == 11:
                            output_weights(T - 1, prev)
                        if e == 13:
                            sum_av(T - 1, prev)

            for T in range(2):
                ln_stats(T, T)
                ln_aggregate(T, T)
                ln_apply(T, T)
            split_y(0, 0)
            gate_dot(0, 0)
            gate_logit(0, 0)
            gate_top(0, 0)
            gate_key_top(0, 0)
            gate_kept(0, 0)
            gate_sum(0, 0)
            gate_rsum(0, 0)
            gate_weights(0, 0)
            ffn_slots(dve, slot)

        @block.scalar
        def _(act):
            def y_squares(T, t):
                act.wait_ge(y_done, T + 1)
                reach(act, ss_min_done, T - 1)
                reach(act, ss_done, T)
                act.activation(y_sq[:], y[:, t % 2], ACT.Square, accum_out=y_ss[:, t % 2:t % 2 + 1]).then_inc(ss_done, 1)

            def split_y(T, t):
                act.wait_ge(yT_tr, T + 1)
                act.activation(yT[:, t % 2, 0], tr[:, 0:C], ACT.Copy).then_inc(yT_hi, 1)

            def split_qk(T, t):
                act.wait_ge(qk_tr, T + 1)
                act.activation(qT[:, 0], tr[:, 0:P], ACT.Copy)
                act.activation(kT[:, t, 0], tr[:, P:2 * P], ACT.Copy).then_inc(qk_hi, 1)

            def gate_exp(T, t):
                act.wait_ge(pool_gate, 9 * T + 3)
                reach(act, kept_done, T)
                act.activation(g_exp[:], gated[:], ACT.Exp, bias=neg_max[:, 0:1]).then_inc(g_exp_done, 1)

            def exponentials(T, t):
                n = (t + 1) * P
                act.wait_ge(scores_ready, T + 1)
                act.wait_ge(sbias_done, T + 1)
                reach(act, p_rsum_done, T)
                act.activation(prob[:, 0:n], sc[:, 0:n], ACT.Exp, bias=s_bias[:, 0:1], scale=SCALE,
                               accum_out=p_sum[:, 0:1]).then_inc(exp_done, 1)

            def split_probs(T, t):
                n = (t + 1) * P
                act.wait_ge(pt_tr, T + 1)
                act.activation(pT[:, 0:t + 1, 0], pt[:, 0:n].rearrange("p (j q) -> p j q", q=P), ACT.Copy).then_inc(pt_hi, 1)

            def split_weights(n):
                raw, hi, lo = weight_halves(n)
                staged(act, n)
                act.activation(hi, raw, ACT.Copy).then_inc(w_hi, 1)

            def slot(T, t):
                for e in range(E):
                    if stage_of(T, e) is not None:
                        split_weights(stage_of(T, e))
                    if e == 0 and inside(T, -1):
                        split_y(T + 1, (t + 1) % QT)
                    if e == 4 and inside(T, 1):
                        split_qk(T - 1, (t + 3) % QT)
                    if e == 5 and inside(T, -2):
                        y_squares(T + 2, (t + 2) % QT)
                    if e == 6 and inside(T, -1):
                        gate_exp(T + 1, (t + 1) % QT)
                    if e == 7 and inside(T, 1):
                        exponentials(T - 1, (t + 3) % QT)
                    if e == 9 and inside(T, 1):
                        split_probs(T - 1, (t + 3) % QT)

            y_squares(0, 0)
            y_squares(1, 1)
            split_y(0, 0)
            gate_exp(0, 0)
            ffn_slots(act, slot)

        @block.gpsimd
        def _(pool):
            def ln_rstd(T, t):
                pool.wait_ge(mv_done, T + 1)
                reach(pool, rstd_done, T)
                settle(pool)
                pool.tensor_scalar(var_eps[:], mv[:, t % 2, 1:2], LN_EPS, None, ALU.add).then_inc(var_done, 1)
                pool.wait_ge(var_done, T + 1)
                reach(pool, y_done, T - 1)
                pool.tensor_tensor(rstd[:, t % 2:t % 2 + 1], var_eps[:], m.power[:, 0:1], ALU.pow).then_inc(rstd_done, 1)

            def y_rnorm(T, t):
                pool.wait_ge(ss_done, T + 1)
                reach(pool, rn_done, T)
                settle(pool)
                pool.tensor_scalar(y_ss_min[:], y_ss[:, t % 2:t % 2 + 1], NORM_MIN ** 2, None, ALU.max).then_inc(ss_min_done, 1)
                pool.wait_ge(ss_min_done, T + 1)
                reach(pool, logit_done, 3 * (T - 2) + 2)
                pool.tensor_tensor(y_rn[:, t % 2:t % 2 + 1], y_ss_min[:], m.power[:, 0:1], ALU.pow).then_inc(rn_done, 1)

            def gate_choice(T, t):
                n = 9 * T
                pool.wait_ge(top_done, T + 1)
                reach(pool, g_exp_done, T)
                reach(pool, kept_done, T)
                settle(pool)
                pool.tensor_scalar(idle[:], top[:, 0:1], 0.0, None, ALU.is_le).then_inc(pool_gate, 1)
                pool.tensor_scalar(neg_max[:], top[:, 0:1], 0.0, -1.0, ALU.max, ALU.mult).then_inc(pool_gate, 1)
                pool.tensor_scalar(gated[:], logit[:], 0.0, None, ALU.max).then_inc(pool_gate, 1)
                pool.tensor_scalar(at_second[:], logit[:], top[:, 1:2], None, ALU.is_ge)
                pool.tensor_scalar(at_first[:], logit[:], top[:, 0:1], None, ALU.is_ge).then_inc(pool_gate, 1)
                pool.wait_ge(pool_gate, n + 4)
                pool.tensor_tensor(at_rank[:], at_second[:], m.rank[:], ALU.mult).then_inc(pool_gate, 1)
                pool.wait_ge(pool_gate, n + 5)
                pool.tensor_tensor(key[:], at_rank[:], at_first[:], ALU.add).then_inc(pool_gate, 1)
                pool.tensor_scalar(active[:], logit[:], 0.0, None, ALU.is_gt).then_inc(pool_gate, 1)

            def gate_chosen(T, t):
                n = 9 * T
                pool.wait_ge(key_top_done, T + 1)
                pool.wait_ge(pool_gate, n + 7)
                settle(pool)
                pool.tensor_scalar(fallback[:], key[:], key_top[:, 1:2], idle[:, 0:1], ALU.is_ge, ALU.mult).then_inc(pool_gate, 1)
                pool.wait_ge(pool_gate, n + 8)
                pool.tensor_tensor(chosen[:], fallback[:], active[:], ALU.add).then_inc(pool_gate, 1)

            def merge_qkv(T, t):
                a = acc[:, t % 2]
                pool.wait_ge(mix_done, E * T + E)
                reach(pool, qk_tr, T)
                pool.tensor_tensor(qkv[:, 0:2 * H], a[:, 0, 0:2 * H], a[:, 1, 0:2 * H], ALU.add).then_inc(merged, 1)
                reach(pool, v_lo, T)
                pool.tensor_tensor(qkv[:, 2 * H:], a[:, 0, 2 * H:], a[:, 1, 2 * H:], ALU.add).then_inc(merged, 1)

            def split_v(T, t):
                pool.wait_ge(merged, 2 * T + 2)
                settle(pool)
                pool.tensor_copy(v[:, t, 0], qkv[:, 2 * H:]).then_inc(v_hi, 1)
                pool.wait_ge(v_hi, T + 1)
                pool.tensor_tensor(v[:, t, 1], qkv[:, 2 * H:], as_f32(v[:, t, 0]), ALU.subtract).then_inc(v_lo, 1)

            def split_av(T, t):
                pool.wait_ge(av_done, T + 1)
                settle(pool)
                pool.tensor_copy(avT[:, t % 2, 0], av[:]).then_inc(av_hi, 1)
                pool.wait_ge(av_hi, T + 1)
                pool.tensor_tensor(avT[:, t % 2, 1], av[:], as_f32(avT[:, t % 2, 0]), ALU.subtract).then_inc(av_lo, 1)

            def merge_x(T, t):
                pool.wait_ge(out_done, OG * T + OG)
                x = tile_of(m.x, T)
                pool.tensor_tensor(x, x, odd[:, t % 2], ALU.add).then_inc(x_merged, 1)

            def slot(T, t):
                nxt, prev, nn = (t + 1) % QT, (t + 3) % QT, (t + 2) % QT
                if inside(T, 1):
                    merge_qkv(T - 1, prev)
                    split_v(T - 1, prev)
                if inside(T, -2):
                    ln_rstd(T + 2, nn)
                if inside(T, -1):
                    gate_choice(T + 1, nxt)
                if inside(T, -2):
                    y_rnorm(T + 2, nn)
                if inside(T, -1):
                    gate_chosen(T + 1, nxt)
                if inside(T, 1):
                    split_av(T - 1, prev)
                if inside(T, 2):
                    merge_x(T - 2, nn)

            for T in range(2):
                ln_rstd(T, T)
            for T in range(2):
                y_rnorm(T, T)
            gate_choice(0, 0)
            gate_chosen(0, 0)
            ffn_slots(pool, slot)



HL = 2
K_COLS = GROUPS * D
PT_STEP = 3 * P
PT_COLS = 15 * P
PROB_AT = (0, P, 3 * P, 6 * P)
PROB_COLS = 10 * P


def load_attention_weights(nc, wq, wk, wv, wd, w_q, w_kv, w_dense):
    cols = 1024
    kv = w_kv.rearrange("(k p) n -> p k n", p=P)
    q = w_q.rearrange("(k p) n -> p k n", p=P)
    dense = w_dense.rearrange("(h p) c -> p h c", p=P)
    per = cols // C
    pieces = [(kv[:, k, 0:K_COLS], wk, k, 0, K_COLS) for k in range(CK)]
    pieces += [(kv[:, k, K_COLS:], wv, k, 0, K_COLS) for k in range(CK)]
    pieces += [(q[:, k, n:n + cols], wq, k, n, cols) for n in range(0, HEADS * D, cols) for k in range(CK)]
    pieces += [(dense[:, h:h + per, :], wd, 0, h * C, cols) for h in range(0, HEADS, per)]
    slots = 8
    with ExitStack() as ctx:
        stage = ctx.enter_context(nc.sbuf_tensor("attn_weight_stage", [P, slots, cols], F32))
        loaded = [ctx.enter_context(nc.semaphore(f"aw_loaded{i}")) for i in range(slots)]
        hi = ctx.enter_context(nc.semaphore("aw_hi"))
        lo = ctx.enter_context(nc.semaphore("aw_lo"))
        block = ctx.enter_context(nc.Block())

        @block.sync
        def _(sp):
            for n, (src, _, _, _, width) in enumerate(pieces):
                reach(sp, lo, n - slots + 1)
                dst = stage[:, n % slots, 0:width]
                if len(src.shape) == 3:
                    dst = dst.rearrange("p (h c) -> p h c", c=C)
                sp.dma_start(dst, src).then_inc(loaded[n % slots], 16)

        @block.scalar
        def _(act):
            for n, (_, dst, k, at, width) in enumerate(pieces):
                act.wait_ge(loaded[n % slots], 16 * (n // slots + 1))
                act.activation(dst[:, 0, k, at:at + width], stage[:, n % slots, 0:width], ACT.Copy).then_inc(hi, 1)

        @block.vector
        def _(dve):
            for n, (_, dst, k, at, width) in enumerate(pieces):
                dve.wait_ge(hi, n + 1)
                dve.tensor_tensor(dst[:, 1, k, at:at + width], stage[:, n % slots, 0:width],
                                  as_f32(dst[:, 0, k, at:at + width]), ALU.subtract).then_inc(lo, 1)


def projections(h):
    if h == 14:
        return {"B": ("q", 15), "C": ("z", 0), "D": ("z", 1), "E": ("z", 2), "F": ("z", 3)}
    if h == 15:
        return {"C": ("q", 0), "E": ("k", 0)}
    extra = {0: {"C": ("v", 0, 0), "D": ("v", 0, 1), "E": ("v", 0, 2)}, 1: {"C": ("v", 0, 3)}, 2: {"E": ("k", 1)},
             3: {"E": ("v", 1, 0)}, 4: {"E": ("v", 1, 1)}, 5: {"E": ("v", 1, 2)}, 6: {"E": ("v", 1, 3)},
             7: {"E": ("k", 2)}, 11: {"E": ("k", 3)}}
    return {"B": ("q", h + 1)} | extra.get(h, {})


PROLOGUE = [("z", 0), ("z", 1), ("z", 2), ("z", 3), ("q", 0), ("k", 0)]
NEXT_ITEM = [("z", 0), ("z", 1), ("z", 2), ("z", 3), ("q", 0), ("k", 0)]
USES = [(h, place, what) for h in range(HEADS) for place, what in sorted(projections(h).items())]
ITEM_USES = len(USES)


def use_index(b, h, place):
    n = [i for i, (uh, up, _) in enumerate(USES) if (uh, up) == (h, place)][0]
    return len(PROLOGUE) + ITEM_USES * b + n


def use_of(b, what):
    if what in NEXT_ITEM:
        return len(PROLOGUE) + ITEM_USES * (b - 1) + [w for _, _, w in USES].index(what) if not (
            isinstance(b, int) and b == 0) else PROLOGUE.index(what)
    return len(PROLOGUE) + ITEM_USES * b + [w for _, _, w in USES].index(what)


def attention_slots(slot):
    def run(eng):
        for h in range(HEADS):
            slot(0, h)
        with eng.Fori(1, B - 1) as b:
            for h in range(HEADS):
                slot(b, h)
        for h in range(HEADS):
            slot(B - 1, h)
        slot(B, 0)
        slot(B, 1)
    return run


def turn_of(i):
    return QT - 1 - i


def unit(b, h, lag):
    item, head = (b, h - lag) if h >= lag else (b - 1, h - lag + HEADS)
    number = item * HEADS + head
    if isinstance(b, int) and not 0 <= number < B * HEADS:
        return None
    return item, head, number


def attention(nc, m, w_q, w_kv, w_dense, out):
    with ExitStack() as ctx:
        def sb(n, shape, dt=F32):
            return ctx.enter_context(nc.sbuf_tensor(f"attn_{n}", shape, dt))

        def ps(n):
            return ctx.enter_context(nc.psum_tensor(f"attn_{n}", [P, 512], F32))

        def sem(n):
            return ctx.enter_context(nc.semaphore(f"attn_{n}"))

        wq = sb("wq", [P, HL, CK, HEADS * D], F32R)
        wk = sb("wk", [P, HL, CK, K_COLS], F32R)
        wv = sb("wv", [P, HL, CK, K_COLS], F32R)
        wd = sb("wd", [P, HL, 1, HEADS * C], F32R)
        load_attention_weights(nc, wq, wk, wv, wd, w_q, w_kv, w_dense)

        stats = sb("ln_stats", [P, QT, 6])
        mv = sb("ln_mean_var", [P, QT, 2])
        var_eps = sb("ln_var_eps", [P, QT])
        rstd = sb("ln_rstd", [P, QT])
        z = sb("z", [P, QT, C])
        zT = sb("zT", [P, HL, CK, SEQ], F32R)
        kT = sb("kT", [P, GROUPS, HL, SEQ], F32R)
        v = sb("v", [P, QT, HL, K_COLS], F32R)
        qT = sb("qT", [P, 2, HL, SEQ], F32R)
        s_bias = sb("score_neg_max", [P, 2, QT])
        p_sum = sb("prob_sum", [P, 2, QT])
        p_rsum = sb("prob_rsum", [P, 2, QT])
        expo = sb("exponentials", [P, PROB_COLS])
        prob = sb("probs", [P, PROB_COLS])
        pT = sb("probsT", [P, HL, PT_COLS], F32R)
        cT = sb("ctxT", [P, 2, HL, SEQ], F32R)

        pj = ps("projections")
        sc = [ps("scores0"), ps("scores1")]
        pt = [ps("turned0"), ps("turned1")]
        cx = ps("ctx")
        dn = [ps("dense0"), ps("dense1")]

        stats_done, mv_done, var_done, rstd_done, z_done = sem("stats"), sem("mv"), sem("var_eps"), sem("rstd"), sem("z")
        zeroed = sem("zeroed")
        pj_ready, pj_hi, pj_lo = sem("pj_ready"), sem("pj_hi"), sem("pj_lo")
        s_ready, s_max, e_done, r_done = sem("s_ready"), sem("s_max"), sem("exp"), sem("rsum")
        wide_done, p_done = sem("wide_prob"), sem("prob")
        t_ready, t_hi, t_lo = sem("t_ready"), sem("t_hi"), sem("t_lo")
        c_ready, c_hi, c_lo = sem("c_ready"), sem("c_hi"), sem("c_lo")
        d_ready, x_added, stored = sem("d_ready"), sem("x_added"), sem("stored")
        block = ctx.enter_context(nc.Block())

        def use_halves(what):
            if what[0] == "z":
                t = what[1]
                return (pj[:, 0:C].rearrange("p (k n) -> p k n", k=CK), zT[:, 0, :, t * P:(t + 1) * P],
                        zT[:, 1, :, t * P:(t + 1) * P])
            if what[0] == "q":
                return pj[:], qT[:, what[1] % 2, 0], qT[:, what[1] % 2, 1]
            if what[0] == "k":
                return pj[:], kT[:, what[1], 0], kT[:, what[1], 1]
            pair, j = what[1:]
            at = slice(pair * 2 * D, (pair + 1) * 2 * D)
            return pj[:, 0:2 * D], v[:, j, 0, at], v[:, j, 1, at]

        def turned(half, i):
            if i == 0:
                return pT[:, half, 0:P].rearrange("p (j q) -> p j q", q=P)
            return pT[:, half, i * P:i * P + (i + 1) * PT_STEP].rearrange("p (j q) -> p j q", q=PT_STEP)[:, :, 0:P]

        def normalised(eng, n, i):
            if i == QT - 1:
                reach(eng, wide_done, n + 1)
            else:
                reach(eng, p_done, (QT - 1) * n + turn_of(i))

        def has_projection(b, h, what):
            return not (isinstance(b, int) and (b == B or (b == B - 1 and h >= 14 and what in NEXT_ITEM)))

        @block.sync
        def _(sp):
            if out is not None:
                out_rows = out.rearrange("b (t p) c -> b p t c", p=P)
                with sp.Fori(0, B) as b:
                    sp.wait_ge(x_added, b * 2 + 2)
                    sp.dma_start(out_rows[bass.ds(b, 1)].rearrange("a p t c -> p (a t) c"),
                                 m.x[:, bass.ds(b * QT, QT), :]).then_inc(stored, 16)
                sp.wait_ge(stored, 16 * B)

        @block.tensor
        def _(pe):
            def product(out_ap, stationary, moving, first, last):
                for n, (a, c) in enumerate(((0, 0), (1, 0), (0, 1))):
                    mm = pe.matmul(out_ap, stationary(a), moving(c), start=first and n == 0, stop=last and n == 2,
                                   skip_group_check=True)
                return mm

            def project(b, n, what):
                reach(pe, pj_lo, n)
                if what[0] == "z":
                    t = what[1]
                    pe.wait_ge(z_done, b * QT + t + 1)
                    for k in range(CK):
                        mm = pe.transpose(pj[:, k * P:(k + 1) * P], z[:, t, k * P:(k + 1) * P], m.ident[:])
                elif what[0] in "qk":
                    w, col = (wq, what[1] * D) if what[0] == "q" else (wk, what[1] * D)
                    for k in range(CK):
                        mm = product(pj[:], lambda a: w[:, a, k, col:col + D], lambda c: zT[:, c, k], k == 0, k == CK - 1)
                else:
                    pair, j = what[1:]
                    for k in range(CK):
                        mm = product(pj[:, 0:2 * D], lambda a: zT[:, a, k, j * P:(j + 1) * P],
                                     lambda c: wv[:, c, k, pair * 2 * D:(pair + 1) * 2 * D], k == 0, k == CK - 1)
                mm.then_inc(pj_ready, 1)

            def scores(u, i):
                b, h, n = u
                if i == QT - 1:
                    pe.wait_ge(pj_lo, use_of(b, ("q", h)) + 1)
                    pe.wait_ge(pj_lo, use_of(b, ("k", h // PER)) + 1)
                reach(pe, e_done, QT * n + turn_of(i) - 1)
                width = max(i + 1, 2) * P
                product(sc[i % 2][:, 0:width], lambda a: qT[:, h % 2, a, i * P:(i + 1) * P],
                        lambda c: kT[:, h // PER, c, 0:width], True, False)
                pe.matmul(sc[i % 2][:, i * P:(i + 1) * P], m.ident_bf[:], m.mask[:], start=False, stop=True,
                          skip_group_check=True).then_inc(s_ready, 1)

            def turn(u, i):
                _, h, n = u
                normalised(pe, n, i)
                reach(pe, t_lo, QT * n + turn_of(i) - 1)
                for j in range(i + 1):
                    at = PROB_AT[i] + j * P
                    mm = pe.transpose(pt[i % 2][:, j * P:(j + 1) * P], prob[:, at:at + P], m.ident[:])
                mm.then_inc(t_ready, 1)

            def attend(u):
                b, h, n = u
                pe.wait_ge(t_lo, QT * n + QT)
                if h == 0:
                    pe.wait_ge(pj_lo, use_of(b, ("v", 0, QT - 1)) + 1)
                if h == HEADS // 2:
                    pe.wait_ge(pj_lo, use_of(b, ("v", 1, QT - 1)) + 1)
                if isinstance(n, int) and n == 0:
                    pe.wait_ge(zeroed, 2)
                reach(pe, c_lo, n)
                g = h // PER
                for j in range(QT):
                    q0 = min(j, 2)
                    at = j * PT_STEP + q0 * P
                    mm = product(cx[:, q0 * P:SEQ], lambda a: v[:, j, a, g * D:(g + 1) * D],
                                 lambda c: pT[:, c, at:at + SEQ - q0 * P], j == 0, j == QT - 1)
                mm.then_inc(c_ready, 1)

            def dense(u, half):
                b, h, n = u
                if half == 0:
                    pe.wait_ge(c_lo, n + 1)
                if h == 0:
                    reach(pe, x_added, 2 * b - 1 + half)
                for t in (2 * half, 2 * half + 1):
                    mm = product(dn[half][:, (t % 2) * C:(t % 2 + 1) * C], lambda a: cT[:, h % 2, a, t * P:(t + 1) * P],
                                 lambda c: wd[:, c, 0, h * C:(h + 1) * C], h == 0 and t % 2 == 0, h == HEADS - 1)
                if h == HEADS - 1:
                    mm.then_inc(d_ready, 1)

            def slot(b, h):
                now, prev, prev2 = unit(b, h, 0), unit(b, h, 1), unit(b, h, 2)

                def place(p):
                    what = projections(h).get(p)
                    if what and has_projection(b, h, what):
                        project(b + 1 if h >= 14 and what in NEXT_ITEM else b, use_index(b, h, p), what)

                if now:
                    scores(now, 3)
                if prev:
                    turn(prev, 3)
                place("B")
                if now:
                    scores(now, 2)
                if prev:
                    turn(prev, 2)
                place("C")
                if prev2:
                    dense(prev2, 0)
                if now:
                    scores(now, 1)
                if prev:
                    turn(prev, 1)
                    turn(prev, 0)
                place("D")
                if now:
                    scores(now, 0)
                if prev2:
                    dense(prev2, 1)
                place("E")
                if prev:
                    attend(prev)
                place("F")

            for n, what in enumerate(PROLOGUE):
                project(0, n, what)
            attention_slots(slot)(pe)

        @block.vector
        def _(dve):
            def layer_norm(b, t):
                T = b * QT + t
                dve.bn_stats(stats[:, t], tile_of(m.x, T)).then_inc(stats_done, 1)
                dve.wait_ge(stats_done, T + 1)
                reach(dve, var_done, T - QT + 1)
                settle(dve)
                dve.bn_aggr(mv[:, t], stats[:, t]).then_inc(mv_done, 1)

            def layer_norm_apply(b, t):
                T = b * QT + t
                dve.wait_ge(rstd_done, T + 1)
                if not (isinstance(b, int) and b == 0):
                    dve.wait_ge(pj_ready, use_of(b - 1, ("z", t)) + 1)
                dve.tensor_scalar(z[:, t], tile_of(m.x, T), mv[:, t, 0:1], rstd[:, t:t + 1],
                                  ALU.subtract, ALU.mult).then_inc(z_done, 1)

            def split(n, what):
                raw, hi, lo = use_halves(what)
                dve.wait_ge(pj_hi, n + 1)
                if what[0] == "q":
                    dve.scalar_tensor_tensor(lo, raw, SCALE, as_f32(hi), ALU.mult, ALU.subtract).then_inc(pj_lo, 1)
                else:
                    dve.tensor_tensor(lo, raw, as_f32(hi), ALU.subtract).then_inc(pj_lo, 1)

            def score_max(u, i):
                _, h, n = u
                dve.wait_ge(s_ready, QT * n + turn_of(i) + 1)
                dve.tensor_reduce(s_bias[:, h % 2, i:i + 1], sc[i % 2][:, 0:(i + 1) * P], AX.X, ALU.max,
                                  negate=True).then_inc(s_max, 1)

            def prob_rsum(u, i):
                _, h, n = u
                dve.wait_ge(e_done, QT * n + turn_of(i) + 1)
                dve.reciprocal(p_rsum[:, h % 2, i:i + 1], p_sum[:, h % 2, i:i + 1]).then_inc(r_done, 1)

            def normalise(u, i):
                _, h, n = u
                dve.wait_ge(r_done, QT * n + turn_of(i) + 1)
                reach(dve, t_ready, QT * (n - 1) + turn_of(i) + 1)
                at, width = PROB_AT[i], (i + 1) * P
                dve.tensor_scalar(prob[:, at:at + width], expo[:, at:at + width], p_rsum[:, h % 2, i:i + 1], None,
                                  ALU.mult).then_inc(p_done, 1)

            def split_turned(u, i):
                _, h, n = u
                dve.wait_ge(t_hi, QT * n + turn_of(i) + 1)
                dve.tensor_tensor(turned(1, i), pt[i % 2][:, 0:(i + 1) * P].rearrange("p (j q) -> p j q", q=P),
                                  as_f32(turned(0, i)), ALU.subtract).then_inc(t_lo, 1)

            def split_context(u):
                _, h, n = u
                dve.wait_ge(c_hi, n + 1)
                dve.tensor_tensor(cT[:, h % 2, 1], cx[:], as_f32(cT[:, h % 2, 0]), ALU.subtract).then_inc(c_lo, 1)

            def add_to_x(b):
                for half in range(2):
                    dve.wait_ge(d_ready, 2 * b + half + 1)
                    x = m.x[:, bass.ds(b * QT + 2 * half, 2), :].rearrange("p t c -> p (t c)") if not isinstance(b, int) \
                        else m.x[:, b * QT + 2 * half:b * QT + 2 * half + 2, :].rearrange("p t c -> p (t c)")
                    dve.tensor_tensor(x, x, dn[half][:], ALU.add).then_inc(x_added, 1)

            def slot(b, h):
                now, prev, prev2 = unit(b, h, 0), unit(b, h, 1), unit(b, h, 2)

                def place(p):
                    what = projections(h).get(p)
                    if what and has_projection(b, h, what):
                        split(use_index(b, h, p), what)

                if now:
                    score_max(now, 3)
                if prev2:
                    split_context(prev2)
                if prev:
                    split_turned(prev, 3)
                if now:
                    prob_rsum(now, 3)
                    score_max(now, 2)
                place("B")
                if prev:
                    split_turned(prev, 2)
                place("C")
                if now:
                    prob_rsum(now, 2)
                    score_max(now, 1)
                if prev:
                    split_turned(prev, 1)
                if now:
                    normalise(now, 2)
                if prev:
                    split_turned(prev, 0)
                place("D")
                if now:
                    prob_rsum(now, 1)
                    score_max(now, 0)
                    normalise(now, 1)
                    prob_rsum(now, 0)
                    normalise(now, 0)
                place("E")
                if not (isinstance(b, int) and b >= B - 1):
                    if 8 <= h < 12:
                        layer_norm(b + 1, h - 8)
                    if 9 <= h < 13:
                        layer_norm_apply(b + 1, h - 9)
                place("F")
                if h == 1 and prev2:
                    add_to_x(b - 1)

            for t in range(QT):
                layer_norm(0, t)
            for t in range(QT):
                layer_norm_apply(0, t)
            for n, what in enumerate(PROLOGUE):
                split(n, what)
            attention_slots(slot)(dve)

        @block.scalar
        def _(act):
            def split(n, what):
                raw, hi, _ = use_halves(what)
                act.wait_ge(pj_ready, n + 1)
                act.activation(hi, raw, ACT.Copy, scale=SCALE if what[0] == "q" else 1.0).then_inc(pj_hi, 1)

            def exponential(u, i):
                _, h, n = u
                act.wait_ge(s_max, QT * n + turn_of(i) + 1)
                normalised(act, n - 1, i)
                at, width = PROB_AT[i], (i + 1) * P
                act.activation(expo[:, at:at + width], sc[i % 2][:, 0:width], ACT.Exp, bias=s_bias[:, h % 2, i:i + 1],
                               accum_out=p_sum[:, h % 2, i:i + 1]).then_inc(e_done, 1)

            def normalise(u, i):
                _, h, n = u
                act.wait_ge(r_done, QT * n + turn_of(i) + 1)
                reach(act, t_ready, QT * (n - 1) + turn_of(i) + 1)
                at, width = PROB_AT[i], (i + 1) * P
                act.activation(prob[:, at:at + width], expo[:, at:at + width], ACT.Copy,
                               scale=p_rsum[:, h % 2, i:i + 1]).then_inc(wide_done, 1)

            def split_turned(u, i):
                _, h, n = u
                act.wait_ge(t_ready, QT * n + turn_of(i) + 1)
                act.activation(turned(0, i), pt[i % 2][:, 0:(i + 1) * P].rearrange("p (j q) -> p j q", q=P),
                               ACT.Copy).then_inc(t_hi, 1)

            def split_context(u):
                _, h, n = u
                act.wait_ge(c_ready, n + 1)
                act.activation(cT[:, h % 2, 0], cx[:], ACT.Copy).then_inc(c_hi, 1)

            def slot(b, h):
                now, prev, prev2 = unit(b, h, 0), unit(b, h, 1), unit(b, h, 2)

                def place(p):
                    what = projections(h).get(p)
                    if what and has_projection(b, h, what):
                        split(use_index(b, h, p), what)

                if prev2:
                    split_context(prev2)
                if prev:
                    split_turned(prev, 3)
                if now:
                    exponential(now, 3)
                place("B")
                if prev:
                    split_turned(prev, 2)
                if now:
                    exponential(now, 2)
                    normalise(now, 3)
                place("C")
                if prev:
                    split_turned(prev, 1)
                if now:
                    exponential(now, 1)
                if prev:
                    split_turned(prev, 0)
                place("D")
                if now:
                    exponential(now, 0)
                place("E")
                place("F")

            for n, what in enumerate(PROLOGUE):
                split(n, what)
            attention_slots(slot)(act)

        @block.gpsimd
        def _(pool):
            def ln_rstd(b, t):
                T = b * QT + t
                pool.wait_ge(mv_done, T + 1)
                reach(pool, rstd_done, T - QT + 1)
                settle(pool)
                pool.tensor_scalar(var_eps[:, t:t + 1], mv[:, t, 1:2], LN_EPS, None, ALU.add).then_inc(var_done, 1)
                pool.wait_ge(var_done, T + 1)
                reach(pool, z_done, T - QT + 1)
                pool.tensor_tensor(rstd[:, t:t + 1], var_eps[:, t:t + 1], m.power[:, 0:1], ALU.pow).then_inc(rstd_done, 1)

            def slot(b, h):
                if 8 <= h < 12 and not (isinstance(b, int) and b >= B - 1):
                    ln_rstd(b + 1, h - 8)

            for half in range(HL):
                at = 3 * PT_STEP + 2 * P
                pool.memset(as_f32(pT[:, half, at:at + P]), 0.0).then_inc(zeroed, 1)
            for t in range(QT):
                ln_rstd(0, t)
            attention_slots(slot)(pool)


def program(nc, inputs, out, parts=("ffn1", "attn", "ffn2")):
    x_in, w_q, w_kv, w_dense, sim_matrix, gates, q_proj, k_proj, v_proj, o_proj = inputs
    with ExitStack() as ctx:
        def sb(n, shape, dt=F32):
            return ctx.enter_context(nc.sbuf_tensor(n, shape, dt))

        m = Resident()
        m.x = sb("x", [P, TILES, C])
        m.ident = sb("ident", [P, P])
        m.ident_bf = sb("ident_bf", [P, P], BF16)
        m.mask = sb("causal_mask", [P, P], BF16)
        m.power = sb("power", [P, E])
        m.rank_i = sb("rank_i", [P, E], mybir.dt.int32)
        m.rank = sb("rank", [P, E])
        m.sig = sb("sigmoid_gates", [P, E])
        m.simw = sb("sim_weights", [P, CK, 2 * E], F32R)
        constants(nc, m, sim_matrix, gates)
        ffn(nc, m, "ffn1", True, q_proj, k_proj, v_proj, o_proj, x_in, None if len(parts) > 1 else out)
        if "attn" in parts:
            attention(nc, m, w_q, w_kv, w_dense, None if "ffn2" in parts else out)
        if "ffn2" in parts:
            ffn(nc, m, "ffn2", False, q_proj, k_proj, v_proj, o_proj, None, out)


_INS = ["L0_attn_x", "L0_attn_w_q", "L0_attn_w_kv", "L0_attn_w_dense", "L0_ffn_sim_matrix", "L0_ffn_gates",
        "L0_ffn_q_proj", "L0_ffn_k_proj", "L0_ffn_v_proj", "L0_ffn_o_proj"]


def kernel(**inputs):
    import numpy as _np
    import concourse.bacc as _bacc
    from concourse import mybir as _mybir
    from concourse.bass_utils import run_bass_kernel_spmd as _run

    nc = _bacc.Bacc("TRN2", target_bir_lowering=False, num_devices=1)
    arrays, args = {}, []
    for name in _INS:
        a = _np.ascontiguousarray(inputs[name])
        arrays[f"in_{name}_dram"] = a
        args.append(nc.dram_tensor(f"in_{name}_dram", a.shape, _mybir.dt.from_np(a.dtype), kind="ExternalInput").ap())
    out = nc.dram_tensor("out_0_dram", (B, SEQ, C), F32, kind="ExternalOutput").ap()
    program(nc, args, out)
    r = _run(nc, [arrays], core_ids=[0])
    return r.results[0]["out_0_dram"]
```
